# Optimizing a Trainium2 kernel written in Bass

```python
import numpy as np
import jax
import jax.numpy as jnp

def _softmax(x, axis=-1):
    return jax.nn.softmax(x, axis=axis)

def _gelu(x):
    return jax.nn.gelu(x, approximate=True)

def _silu(x):
    return jax.nn.silu(x)

def _sigmoid(x):
    return jax.nn.sigmoid(x)

def _layernorm(x, axis=-1, eps=1e-05):
    m = jnp.mean(x, axis=axis, keepdims=True)
    v = jnp.var(x, axis=axis, keepdims=True)
    return (x - m) / jnp.sqrt(v + eps)

def _scatter_add(tgt, idx, src, axis=0):
    return tgt.at[idx].add(src)

def _segment_sum(src, seg, n):
    return jax.ops.segment_sum(src, seg, n)
kernel_name = 'mk_gnn_resnorm_d4_gnn_r32_349134'

def setup_inputs(seed: int=0):
    np.random.seed(seed)
    _w = jnp.asarray

    def _rec_inputs():
        import jax
        import jax.numpy as jnp
        _gk = jax.random.key(seed)
        x = -0.0006008 + 1.001 * jax.random.normal(jax.random.fold_in(_gk, 1), (50000, 256), jnp.float32)
        src = jax.random.randint(jax.random.fold_in(_gk, 2), (25000,), 0, 50000, jnp.int32)
        dst = jax.random.randint(jax.random.fold_in(_gk, 3), (25000,), 0, 50000, jnp.int32)
        _o = jnp.argsort(dst, stable=True)
        src = src[_o]
        dst = dst[_o]
        edge_attr_256 = 2.93046e-05 + 1.00006 * jax.random.normal(jax.random.fold_in(_gk, 13), (25000, 256), jnp.float32)
        edge_attr_64 = 0.000189758 + 1.00013 * jax.random.normal(jax.random.fold_in(_gk, 14), (25000, 64), jnp.float32)
        return (x, src, dst, edge_attr_256, edge_attr_64)
    x, src, dst, edge_attr_256, edge_attr_64 = _rec_inputs()

    def _L0_gnn_setup():
        import jax, jax.numpy as jnp
        import numpy as np
        N, E, D = (10000, 10000, 256)
        BN_EPS = 1e-05
        key = jax.random.key(seed)
        ks = jax.random.split(key, 9)
        x = jax.random.normal(ks[0], (N, D), dtype=jnp.float32)
        edge_index = jax.random.randint(ks[1], (2, E), 0, N, dtype=jnp.int64)
        edge_embed = jax.random.normal(ks[2], (E, D), dtype=jnp.float32)
        s = 1.0 / np.sqrt(D)
        W1 = jax.random.uniform(ks[3], (D, D), jnp.float32, -s, s)
        b1 = jax.random.uniform(ks[4], (D,), jnp.float32, -s, s)
        gamma = jnp.ones((D,), jnp.float32)
        beta = jnp.zeros((D,), jnp.float32)
        W2 = jax.random.uniform(ks[5], (D, D), jnp.float32, -s, s)
        b2 = jax.random.uniform(ks[6], (D,), jnp.float32, -s, s)
        eps = jnp.zeros((1,), jnp.float32)
        return {'x': x, 'edge_index': edge_index, 'edge_embed': edge_embed, 'W1': W1, 'b1': b1, 'gamma': gamma, 'beta': beta, 'W2': W2, 'b2': b2, 'eps': eps}
    _L0_gnn_all = _L0_gnn_setup()
    _L0_gnn_in = {k: v for k, v in _L0_gnn_all.items() if k in ('W1', 'b1', 'gamma', 'beta', 'W2', 'b2', 'eps')}
    del _L0_gnn_all

    def _L1_gnn_setup():
        import jax, jax.numpy as jnp
        import numpy as np
        N_NODES = 50000
        N_EDGES = 25000
        NODE_IN = 256
        EDGE_OUT = 64
        GLOBAL_IN = 128
        NODE_OUT = 256
        HIDDEN = 512
        N_GRAPHS = 64
        key = jax.random.key(seed)
        ks = jax.random.split(key, 8)
        x = jax.random.normal(ks[0], (N_NODES, NODE_IN), dtype=jnp.float32)
        edge_index = jax.random.randint(ks[1], (2, N_EDGES), 0, N_NODES, dtype=jnp.int64)
        edge_attr = jax.random.normal(ks[2], (N_EDGES, EDGE_OUT), dtype=jnp.float32)
        u = jax.random.normal(ks[3], (N_GRAPHS, GLOBAL_IN), dtype=jnp.float32)
        batch = jnp.sort(jax.random.randint(ks[4], (N_NODES,), 0, N_GRAPHS, dtype=jnp.int64))
        in_dim = NODE_IN + EDGE_OUT + GLOBAL_IN
        b1s = 1.0 / np.sqrt(in_dim)
        b2s = 1.0 / np.sqrt(HIDDEN)
        W1 = jax.random.uniform(ks[5], (in_dim, HIDDEN), dtype=jnp.float32, minval=-b1s, maxval=b1s)
        b1 = jnp.zeros((HIDDEN,), dtype=jnp.float32)
        W2 = jax.random.uniform(ks[6], (HIDDEN, NODE_OUT), dtype=jnp.float32, minval=-b2s, maxval=b2s)
        b2 = jnp.zeros((NODE_OUT,), dtype=jnp.float32)
        return {'x': x, 'edge_index': edge_index, 'edge_attr': edge_attr, 'u': u, 'batch': batch, 'W1': W1, 'b1': b1, 'W2': W2, 'b2': b2}
    _L1_gnn_all = _L1_gnn_setup()
    _L1_gnn_in = {k: v for k, v in _L1_gnn_all.items() if k in ('u', 'W1', 'b1', 'W2', 'b2')}
    del _L1_gnn_all

    def _L2_gnn_setup():
        import jax, jax.numpy as jnp
        import numpy as np
        N, E, IN_DIM, H, D = (50000, 25000, 256, 8, 32)
        ALPHA = 0.2
        key = jax.random.key(seed)
        ks = jax.random.split(key, 6)
        feat = jax.random.normal(ks[0], (N, IN_DIM), dtype=jnp.float32)
        src = jax.random.randint(ks[1], (E,), 0, N, dtype=jnp.int32)
        dst = jax.random.randint(ks[2], (E,), 0, N, dtype=jnp.int32)
        W = jax.random.normal(ks[3], (IN_DIM, H * D), dtype=jnp.float32) * 0.05
        attn_l = jax.random.normal(ks[4], (H, D), dtype=jnp.float32)
        attn_r = jax.random.normal(ks[5], (H, D), dtype=jnp.float32)
        return {'feat': feat, 'src': src, 'dst': dst, 'W': W, 'attn_l': attn_l, 'attn_r': attn_r}
    _L2_gnn_all = _L2_gnn_setup()
    _L2_gnn_in = {k: v for k, v in _L2_gnn_all.items() if k in ('W', 'attn_l', 'attn_r')}
    del _L2_gnn_all

    def _L3_gnn_setup():
        import jax, jax.numpy as jnp
        import numpy as np
        N_NODES = 50000
        N_EDGES = 25000
        F_IN = 256
        HEADS = 4
        C_OUT = 64
        NEG_SLOPE = 0.2
        key = jax.random.key(seed)
        k0, k1, k2, k3, k4, k5 = jax.random.split(key, 6)
        x = jax.random.normal(k0, (N_NODES, F_IN), dtype=jnp.float32)
        edge_index = jax.random.randint(k1, (2, N_EDGES), 0, N_NODES, dtype=jnp.int64)
        s = 1.0 / np.sqrt(F_IN)
        W = jax.random.uniform(k2, (HEADS * C_OUT, F_IN), minval=-s, maxval=s, dtype=jnp.float32)
        att_src = jax.random.normal(k3, (HEADS, C_OUT), dtype=jnp.float32) * 0.1
        att_dst = jax.random.normal(k4, (HEADS, C_OUT), dtype=jnp.float32) * 0.1
        bias = jnp.zeros((HEADS * C_OUT,), dtype=jnp.float32)
        return {'x': x, 'edge_index': edge_index, 'W': W, 'att_src': att_src, 'att_dst': att_dst, 'bias': bias}
    _L3_gnn_all = _L3_gnn_setup()
    _L3_gnn_in = {k: v for k, v in _L3_gnn_all.items() if k in ('W', 'att_src', 'att_dst', 'bias')}
    del _L3_gnn_all
    return {'x': x, 'src': src, 'dst': dst, 'edge_attr_256': edge_attr_256, 'edge_attr_64': edge_attr_64, 'L0_gnn_W1': _L0_gnn_in['W1'], 'L0_gnn_b1': _L0_gnn_in['b1'], 'L0_gnn_gamma': _L0_gnn_in['gamma'], 'L0_gnn_beta': _L0_gnn_in['beta'], 'L0_gnn_W2': _L0_gnn_in['W2'], 'L0_gnn_b2': _L0_gnn_in['b2'], 'L0_gnn_eps': _L0_gnn_in['eps'], 'L1_gnn_u': _L1_gnn_in['u'], 'L1_gnn_W1': _L1_gnn_in['W1'], 'L1_gnn_b1': _L1_gnn_in['b1'], 'L1_gnn_W2': _L1_gnn_in['W2'], 'L1_gnn_b2': _L1_gnn_in['b2'], 'L2_gnn_W': _L2_gnn_in['W'], 'L2_gnn_attn_l': _L2_gnn_in['attn_l'], 'L2_gnn_attn_r': _L2_gnn_in['attn_r'], 'L3_gnn_W': _L3_gnn_in['W'], 'L3_gnn_att_src': _L3_gnn_in['att_src'], 'L3_gnn_att_dst': _L3_gnn_in['att_dst'], 'L3_gnn_bias': _L3_gnn_in['bias']}

def reference(x, src, dst, edge_attr_256, edge_attr_64, L0_gnn_W1, L0_gnn_b1, L0_gnn_gamma, L0_gnn_beta, L0_gnn_W2, L0_gnn_b2, L0_gnn_eps, L1_gnn_u, L1_gnn_W1, L1_gnn_b1, L1_gnn_W2, L1_gnn_b2, L2_gnn_W, L2_gnn_attn_l, L2_gnn_attn_r, L3_gnn_W, L3_gnn_att_src, L3_gnn_att_dst, L3_gnn_bias):
    import jax
    import jax.numpy as jnp

    def _L0_gnn_ref(x, edge_index, edge_embed, W1, b1, gamma, beta, W2, b2, eps):
        import jax, jax.numpy as jnp
        import numpy as np
        N, E, D = (10000, 10000, 256)
        BN_EPS = 1e-05
        row, col = (edge_index[0], edge_index[1])
        msg = x[col] * edge_embed
        agg = jax.ops.segment_sum(msg, row, num_segments=x.shape[0])
        h = (1.0 + eps) * x + agg
        h1 = h @ W1 + b1
        mean = jnp.mean(h1, axis=0)
        var = jnp.mean(jnp.square(h1 - mean), axis=0)
        h1 = (h1 - mean) * jax.lax.rsqrt(var + BN_EPS) * gamma + beta
        h1 = jax.nn.relu(h1)
        return h1 @ W2 + b2

    def _L1_gnn_ref(x, edge_index, edge_attr, u, batch, W1, b1, W2, b2):
        import jax, jax.numpy as jnp
        import numpy as np
        N_NODES = 50000
        N_EDGES = 25000
        NODE_IN = 256
        EDGE_OUT = 64
        GLOBAL_IN = 128
        NODE_OUT = 256
        HIDDEN = 512
        N_GRAPHS = 64
        n = x.shape[0]
        src = edge_index[0]
        sums = jax.ops.segment_sum(edge_attr, src, num_segments=n)
        counts = jax.ops.segment_sum(jnp.ones((edge_attr.shape[0],), edge_attr.dtype), src, num_segments=n)
        edge_attr_agg = sums / jnp.maximum(counts, 1.0)[:, None]
        u_expanded = u[batch]
        combined = jnp.concatenate([x, edge_attr_agg, u_expanded], axis=1)
        h = jax.nn.relu(combined @ W1 + b1)
        return h @ W2 + b2

    def _L2_gnn_ref(feat, src, dst, W, attn_l, attn_r):
        import jax, jax.numpy as jnp
        import numpy as np
        N, E, IN_DIM, H, D = (50000, 25000, 256, 8, 32)
        ALPHA = 0.2
        n = feat.shape[0]
        ft = (feat @ W).reshape(n, H, D)
        a1 = jnp.einsum('nhd,hd->nh', ft, attn_l)
        a2 = jnp.einsum('nhd,hd->nh', ft, attn_r)
        e = jax.nn.leaky_relu(a1[src] + a2[dst], negative_slope=ALPHA)
        m = jax.ops.segment_max(e, dst, num_segments=n)
        ex = jnp.exp(e - m[dst])
        s = jax.ops.segment_sum(ex, dst, num_segments=n)
        alpha = ex / s[dst]
        msg = ft[src] * alpha[:, :, None]
        out = jax.ops.segment_sum(msg, dst, num_segments=n)
        return jax.nn.elu(out.reshape(n, H * D))

    def _L3_gnn_ref(x, edge_index, W, att_src, att_dst, bias):
        import jax, jax.numpy as jnp
        import numpy as np
        N_NODES = 50000
        N_EDGES = 25000
        F_IN = 256
        HEADS = 4
        C_OUT = 64
        NEG_SLOPE = 0.2
        N = x.shape[0]
        H, C = att_src.shape
        loops = jnp.arange(N, dtype=edge_index.dtype)
        src = jnp.concatenate([edge_index[0], loops])
        dst = jnp.concatenate([edge_index[1], loops])
        h = (x @ W.T).reshape(N, H, C)
        a_s = jnp.einsum('nhc,hc->nh', h, att_src)
        a_d = jnp.einsum('nhc,hc->nh', h, att_dst)
        e = jax.nn.leaky_relu(a_s[src] + a_d[dst], NEG_SLOPE)
        m = jax.ops.segment_max(e, dst, num_segments=N)
        m = jnp.where(jnp.isfinite(m), m, 0.0)
        p = jnp.exp(e - m[dst])
        denom = jax.ops.segment_sum(p, dst, num_segments=N)
        alpha = p / (denom[dst] + 1e-16)
        msg = alpha[:, :, None] * h[src]
        out = jax.ops.segment_sum(msg, dst, num_segments=N)
        out = out.reshape(N, H * C) + bias
        out = jax.nn.elu(out) + x
        return out
    edge_index = jnp.stack([src, dst])
    batch0 = jnp.zeros((50000,), jnp.int32)
    x = _layernorm(x + _L0_gnn_ref(x, edge_index, edge_attr_256, L0_gnn_W1, L0_gnn_b1, L0_gnn_gamma, L0_gnn_beta, L0_gnn_W2, L0_gnn_b2, L0_gnn_eps), axis=-1)
    x = _layernorm(x + _L1_gnn_ref(x, edge_index, edge_attr_64, L1_gnn_u, batch0, L1_gnn_W1, L1_gnn_b1, L1_gnn_W2, L1_gnn_b2), axis=-1)
    x = _layernorm(x + _L2_gnn_ref(x, src, dst, L2_gnn_W, L2_gnn_attn_l, L2_gnn_attn_r), axis=-1)
    x = _layernorm(x + _L3_gnn_ref(x, edge_index, L3_gnn_W, L3_gnn_att_src, L3_gnn_att_dst, L3_gnn_bias), axis=-1)
    return x

_drawn_inputs = setup_inputs


def setup_inputs(seed=0):
    import zlib

    import numpy as np

    out = dict(_drawn_inputs(seed))
    spreads = {'L0_gnn_gamma': (1.0, 0.2),
     'L0_gnn_beta': (0.0, 0.1),
     'L1_gnn_b1': (0.0, 0.1),
     'L1_gnn_b2': (0.0, 0.1),
     'L3_gnn_bias': (0.0, 0.1)}
    factors = {'L0_gnn_b1': 8.0, 'L2_gnn_attn_r': 2.764, 'L3_gnn_att_src': 3.07, 'L3_gnn_att_dst': 7.865}
    for name, (base, spread) in spreads.items():
        noise = np.random.default_rng([zlib.crc32(name.encode()), seed]).standard_normal(out[name].shape)
        drawn = base * np.exp(spread * noise) if base else spread * noise
        out[name] = jnp.asarray(drawn.astype(out[name].dtype))
    for name, factor in factors.items():
        out[name] = (out[name] * factor).astype(out[name].dtype)
    return out
```

```python
import concourse.bass as bass
from concourse import mybir
from contextlib import ExitStack


class Step:

    def __init__(self, s, b, n):
        self.s, self.b, self.n = s, b, n

    def plus(self, d):
        t = self.b + d
        return Step(self.s + d, t % 2, self.n + t // 2)

    def known(self):
        return isinstance(self.s, int)


def run_steps(eng, total, body, start=0, peel=2):
    first, last = (start + peel + 1) // 2, (start + total - 2) // 2
    for s in range(start, 2 * first):
        body(Step(s, s % 2, s // 2))
    with eng.Fori(first, last) as n:
        body(Step(2 * n, 0, n))
        body(Step(2 * n + 1, 1, n))
    for s in range(2 * last, start + total):
        body(Step(s, s % 2, s // 2))


def at(s):
    return Step(s, s % 2, s // 2)


def wait(eng, sem, value):
    if not isinstance(value, int) or value > 0:
        eng.wait_ge(sem, value)


def gnn_program(nc, x, src, dst, ea256, ea64,
                w1_0, b1_0, gamma_0, beta_0, w2_0, b2_0, eps_0,
                u_1, w1_1, b1_1, w2_1, b2_1,
                w_2, al_2, ar_2, w_3, as_3, ad_3, bias_3, out, stop_after=9):
    F32, I32 = mybir.dt.float32, mybir.dt.int32
    ALU = mybir.AluOpType
    ACT = mybir.ActivationFunctionType
    AXX = mybir.AxisListType.X
    P = 128
    N, D = x.shape
    E, DE = ea64.shape
    HID = w1_1.shape[1]
    H2, H3 = al_2.shape[0], as_3.shape[0]
    FH = D // P
    KH = HID // P
    J = 4
    STEP = P * J
    BIG = 1.0e30
    LN_EPS = 1e-5
    SLOPE = 0.2
    NS = -(-N // STEP)
    NLAST = (N - (NS - 1) * STEP) // J
    ES = -(-E // STEP)
    ELAST = (E - (ES - 1) * STEP) // J
    assert (NS - 1) * STEP + NLAST * J == N and (ES - 1) * STEP + ELAST * J == E
    C = J * (-(-E // (P * J)))
    EFULL = E // C
    EREM = E - EFULL * C
    CS = C // J
    assert EFULL == P - 1 and EREM > 1
    TROWS = 3 * P * (-(-(N + P + 1) // (3 * P)))
    TW0 = D + DE + 4
    AW = 16
    TW = D + AW
    SC, MC = D, D + AW // 2

    tab0 = nc.dram_tensor("tab0", [TROWS, TW0], F32).ap()
    tab = nc.dram_tensor("tab", [TROWS, TW], F32).ap()
    h1_d = nc.dram_tensor("h1_d", [NS, P, FH, STEP], F32).ap()
    x2_d = nc.dram_tensor("x2_d", [N, D], F32).ap()
    x3_d = nc.dram_tensor("x3_d", [N, D], F32).ap()

    def node_view(t, k, cols=slice(None), start=0):
        if k.known() and k.s - start == NS - 1:
            a = t[(NS - 1) * STEP:N, cols].rearrange("(p j) d -> p j d", j=J)
            return a, NLAST
        a = t[0:(NS - 1) * STEP, cols].rearrange("(s p j) d -> s p j d", p=P, j=J)
        return a[k.s - start, :, :, :], P

    def live(k, total):
        return not (k.known() and k.s >= total)

    ctx = ExitStack()
    with ctx:
        def sb(name, shape, dt=F32):
            return ctx.enter_context(nc.sbuf_tensor(name, shape, dt))

        def sem(name):
            return ctx.enter_context(nc.semaphore(name))

        ident = sb("ident", [P, P])
        lower = sb("lower", [P, P])
        trash = sb("trash", [P, 1])
        zero = sb("zero", [P, 3 * TW0])
        W1a = sb("W1a", [P, FH, D])
        W2a = sb("W2a", [P, FH, D])
        W1b = sb("W1b", [P, FH, HID])
        W1e = sb("W1e", [DE, HID])
        W1u = sb("W1u", [P, HID])
        W2b = sb("W2b", [P, KH, D])
        Wg = {2: sb("Wg2", [P, FH, D + 2 * H2]), 3: sb("Wg3", [P, FH, D + 2 * H3])}
        colv = sb("colv", [P, 3, FH])
        b1col = sb("b1col", [P, KH])
        u0 = sb("u0", [P, 1])
        hbias = sb("hbias", [P, KH])
        b2a = sb("b2a", [P, D])
        b2b = sb("b2b", [P, D])
        bias3 = sb("bias3", [P, D])
        att = {2: sb("att2", [P, 2, D]), 3: sb("att3", [P, 2, D])}
        onepe = sb("onepe", [P, 1])
        expo = sb("expo", [P, J])
        lneps = sb("lneps", [P, J])
        hold = sb("hold", [P, 5])
        bnA = sb("bnA", [P, FH])
        bnB = sb("bnB", [P, FH])
        IDX = sb("IDX", [P, 3, C], I32)
        NEG = sb("NEG", [P, C])
        CT = sb("CT", [P, P])
        fixg = sb("fixg", [P, 1], I32)
        fixs = sb("fixs", [P, 1], I32)

        ARENA = 32 * 1024
        arena = sb("arena", [P, ARENA])
        cursor = [0]

        def take(shape, dt=F32, parts=P):
            n = 1
            for d in shape:
                n *= d
            n += n % 2
            a = arena[0:parts, cursor[0]:cursor[0] + n]
            cursor[0] += n
            assert cursor[0] <= ARENA, cursor[0]
            if dt != F32:
                a = a.bitcast(dt)
            if len(shape) > 1:
                names = "abcd"[:len(shape)]
                pat = " ".join(names)
                m = 1
                for d in shape:
                    m *= d
                a = a[:, 0:m].rearrange(f"p ({pat}) -> p {pat}", **{c: d for c, d in zip(names, shape)})
            return a

        def fresh():
            cursor[0] = 0

        psum = ctx.enter_context(nc.psum_tensor("psum", [P, 8, 512], F32))

        s_phase = sem("s_phase")
        s_c = {k: sem(f"s_c_{k}") for k in ("id", "w", "wg3", "ps", "misc", "prep", "fill0", "fill1")}

        s_hold = [sem(f"s_hold{i}") for i in range(4)]

        block = ctx.enter_context(nc.Block())
        programs = {"sync": [], "gpsimd": [], "vector": [], "scalar": [], "tensor": []}
        phases = [0]

        PHASES = []

        def barrier(eng, k):
            eng.drain().then_inc(s_phase, 1)
            eng.wait_ge(s_phase, 5 * k)

        fresh()
        srcI = take([ES, J], I32)
        dstI = take([ES, J], I32)
        xg = take([2, J, D])
        eat = take([2, J, D])
        msg = take([2, J, TW0])
        comb = take([2, J, TW0])
        same = take([2, J, P])
        srcF = take([2, J])
        gidx = take([2, J], I32)
        sidx = take([2, J], I32)
        cnt = take([J])
        fst = take([J])
        fsd = take([J])
        junk = take([J, P])
        lda = take([FH, D])
        mulA = take([FH, D])
        dI = take([C], I32)
        dnI = take([C], I32)
        dF = take([C])
        dnF = take([C])
        sS = take([C], I32)
        lastF = take([C])
        edge1 = {k: sem(f"e1_{k}") for k in
                 ("idx", "pad", "ones", "gix", "srcF", "srow", "same", "cnt", "first", "d", "sidx", "msg",
                  "csum", "comb", "scat", "prep", "row", "wt")}
        e1_ea = [sem(f"e1_ea{b}") for b in range(2)]
        e1_xg = [sem(f"e1_xg{b}") for b in range(2)]
        q = edge1
        PADROW = N + P
        NFILL = TROWS // (3 * P)

        def p1_sync(sp):
            sp.wait_ge(q["pad"], 2)
            for I, a in ((srcI, src), (dstI, dst)):
                sp.dma_start(I[:, 0:ES - 1, :], a[0:(ES - 1) * STEP].rearrange("(s p j) -> p s j", p=P, j=J)).then_inc(q["idx"], 16)
                sp.dma_start(I[0:ELAST, ES - 1, :], a[(ES - 1) * STEP:E].rearrange("(p j) -> p j", j=J)).then_inc(q["idx"], 16)
            sp.wait_ge(s_c["id"], 1)
            t0 = tab0.rearrange("(k p r) c -> k p (r c)", p=P, r=3)
            with sp.Fori(0, NFILL) as i:
                sp.dma_start(t0[i, :, :], zero[:, :]).then_inc(s_c["fill0"], 16)

            em = ea256[0:(ES - 1) * STEP, :].rearrange("(s p j) d -> s p j d", p=P, j=J)
            fm = ea64[0:(ES - 1) * STEP, :].rearrange("(s p j) d -> s p j d", p=P, j=J)
            sp.wait_ge(q["ones"], 2)

            def body(k):
                wait(sp, q["csum"], J * (k.s - 1))
                if k.known() and k.s == ES - 1:
                    sp.dma_start(eat[0:ELAST, k.b, :, :], ea256[(ES - 1) * STEP:E, :].rearrange("(p j) d -> p j d", j=J)).then_inc(e1_ea[k.b], 16)
                    sp.dma_start(msg[0:ELAST, k.b, :, D:D + DE], ea64[(ES - 1) * STEP:E, :].rearrange("(p j) d -> p j d", j=J)).then_inc(e1_ea[k.b], 16)
                else:
                    sp.dma_start(eat[:, k.b, :, :], em[k.s, :, :, :]).then_inc(e1_ea[k.b], 16)
                    sp.dma_start(msg[:, k.b, :, D:D + DE], fm[k.s, :, :, :]).then_inc(e1_ea[k.b], 16)
            run_steps(sp, ES, body)

        def p1_act_loads(act):
            loads = [(W1a[:, :, :], w1_0.rearrange("(f p) d -> p f d", p=P)),
                     (W2a[:, :, :], w2_0.rearrange("(f p) d -> p f d", p=P)),
                     (W1b[:, :, :], w1_1[0:D, :].rearrange("(f p) d -> p f d", p=P)),
                     (W1e[:, :], w1_1[D:D + DE, :]),
                     (W1u[:, :], w1_1[D + DE:D + DE + P, :]),
                     (W2b[:, :, :], w2_1.rearrange("(f p) d -> p f d", p=P)),
                     (Wg[2][:, :, 0:D], w_2.rearrange("(f p) d -> p f d", p=P)),
                     (lda, w_3.rearrange("(f p) d -> p f d", p=P)),
                     (b2a[:, :], b2_0.rearrange("(a d) -> a d", a=1).to_broadcast([P, D])),
                     (b2b[:, :], b2_1.rearrange("(a d) -> a d", a=1).to_broadcast([P, D])),
                     (bias3[:, :], bias_3.rearrange("(a d) -> a d", a=1).to_broadcast([P, D])),
                     (onepe[:, :], eps_0.rearrange("(a d) -> a d", a=1).to_broadcast([P, 1])),
                     (u0[:, :], u_1[0, :].rearrange("(p a) -> p a", a=1))]
            for i, v in enumerate((b1_0, gamma_0, beta_0)):
                for f in range(FH):
                    loads.append((colv[:, i, f:f + 1], v[f * P:(f + 1) * P].rearrange("(p a) -> p a", a=1)))
            for k in range(KH):
                loads.append((b1col[:, k:k + 1], b1_1[k * P:(k + 1) * P].rearrange("(p a) -> p a", a=1)))
            for L, vs in ((2, (al_2, ar_2)), (3, (as_3, ad_3))):
                for i, v in enumerate(vs):
                    loads.append((att[L][:, i, :], v.rearrange("h d -> (h d)").rearrange("(a n) -> a n", a=1).to_broadcast([P, D])))
            loads += [(dI[0:EFULL, :], dst[0:EFULL * C].rearrange("(p c) -> p c", c=C)),
                      (dI[EFULL:P, 0:EREM], dst[EFULL * C:E].rearrange("(a c) -> a c", a=1)),
                      (dnI[0:EFULL, :], dst[1:EFULL * C + 1].rearrange("(p c) -> p c", c=C)),
                      (dnI[EFULL:P, 0:EREM - 1], dst[EFULL * C + 1:E].rearrange("(a c) -> a c", a=1)),
                      (sS[0:EFULL, :], src[0:EFULL * C].rearrange("(p c) -> p c", c=C)),
                      (sS[EFULL:P, 0:EREM], src[EFULL * C:E].rearrange("(a c) -> a c", a=1))]
            act.wait_ge(q["pad"], 5)
            with nc.allow_non_contiguous_dma(reason="a weight vector a partition each, once"):
                for o, i in loads:
                    act.dma_start(o, i).then_inc(s_c["w"], 16)
            act.wait_ge(s_c["fill0"], 16 * NFILL)
            t1 = tab.rearrange("(k p r) c -> k p (r c)", p=P, r=3)
            with act.Fori(0, NFILL) as i:
                act.dma_start(t1[i, :, :], zero[:, 0:3 * TW]).then_inc(s_c["fill1"], 16)
            return 16 * len(loads)

        nloads = [0]

        def p1_scalar(act):
            nloads[0] = p1_act_loads(act)
            for f in range(FH):
                act.wait_ge(q["wt"], f + 1)
                act.activation(Wg[3][:, f, 0:D], psum[:, 4 + f, 0:D], ACT.Copy).then_inc(s_c["wg3"], 1)
            act.wait_ge(q["wt"], FH + KH)
            for k in range(KH):
                act.activation(hbias[:, k:k + 1], psum[:, 6, k:k + 1], ACT.Identity, bias=b1col[:, k:k + 1]).then_inc(s_c["misc"], 1)

            def body(k):
                for j in range(J):
                    act.wait_ge(q["csum"], J * k.s + j + 1)
                    if j == 0:
                        wait(act, q["scat"], 16 * J * (k.s - 1))
                    act.activation(comb[:, k.b, j, :], psum[:, 2 + j % 2, 0:TW0], ACT.Copy).then_inc(q["comb"], 1)
            run_steps(act, ES, body)

        def settle(pool, site, before):
            wait(pool, s_hold[site], before)
            pool.tensor_tensor(out=hold[:, site + 1:site + 2], in0=hold[:, 0:1], in1=hold[:, 0:1], op=ALU.add).then_inc(s_hold[site], 1)

        def p1_gpsimd(pool):
            pool.memset(srcI[:, ES - 1, :], PADROW).then_inc(q["pad"], 1)
            pool.memset(dstI[:, ES - 1, :], 0).then_inc(q["pad"], 1)
            pool.memset(dI, N).then_inc(q["pad"], 1)
            pool.memset(dnI, N).then_inc(q["pad"], 1)
            pool.memset(sS, 0).then_inc(q["pad"], 1)
            pool.memset(zero[:, :], 0.0).then_inc(s_c["id"], 1)
            pool.memset(hold[:, :], 0.0).then_inc(q["pad"], 1)
            pool.wait_ge(q["pad"], 6)
            pool.memset(ident[:, :], 0.0).then_inc(s_c["id"], 1)
            pool.memset(lower[:, :], 1.0).then_inc(s_c["id"], 1)
            pool.wait_ge(s_c["id"], 3)
            pool.affine_select(out=ident[:, :], in_=ident[:, :], compare_op=ALU.not_equal, fill=1.0, base=0,
                               pattern=[[-1, P]], channel_multiplier=1).then_inc(s_c["id"], 1)
            pool.affine_select(out=lower[:, :], in_=lower[:, :], compare_op=ALU.is_gt, fill=0.0, base=0,
                               pattern=[[-1, P]], channel_multiplier=1).then_inc(s_c["id"], 1)
            pool.iota(trash[:, :], pattern=[[0, 1]], base=N, channel_multiplier=1,
                      allow_small_or_imprecise_dtypes=True).then_inc(s_c["id"], 1)
            pool.memset(expo[:, :], -0.5).then_inc(s_c["id"], 1)
            pool.memset(lneps[:, :], LN_EPS).then_inc(s_c["id"], 1)
            pool.wait_ge(q["idx"], 64)

            def gather(k):
                wait(pool, q["msg"], k.s - 1)
                pool.wait_ge(q["gix"], k.s + 1)
                settle(pool, 0, k.s)
                for j in range(J):
                    pool.indirect_dma_start(out=xg[:, k.b, j, :], out_offset=None, in_=x[:, :],
                                            in_offset=bass.IndirectOffsetOnAxis(ap=gidx[:, k.b, j:j + 1], axis=0)).then_inc(e1_xg[k.b], 16)

            def scatter(k):
                if k.known() and k.s == 0:
                    pool.wait_ge(s_c["fill0"], 16 * NFILL)
                for j in range(J):
                    wait(pool, q["scat"], 16 * (J * k.s + j))
                    pool.wait_ge(q["comb"], J * k.s + j + 1)
                    if j == 0:
                        pool.wait_ge(q["sidx"], k.s + 1)
                    settle(pool, 1, J * k.s + j)
                    pool.indirect_dma_start(out=tab0[:, :], out_offset=bass.IndirectOffsetOnAxis(ap=sidx[:, k.b, j:j + 1], axis=0),
                                            in_=comb[:, k.b, j, :], in_offset=None, compute_op=ALU.add).then_inc(q["scat"], 16)

            gather(Step(0, 0, 0))

            def body(k):
                nxt = k.plus(1)
                if not (nxt.known() and nxt.s >= ES):
                    gather(nxt)
                scatter(k)
            run_steps(pool, ES, body)
            pool.wait_ge(q["scat"], 16 * J * ES)

        def p1_vector(v):
            v.memset(msg, 1.0).then_inc(q["ones"], 1)
            v.memset(eat, 1.0).then_inc(q["ones"], 1)
            v.wait_ge(s_c["id"], 8)
            v.wait_ge(q["idx"], 64)
            v.wait_ge(s_c["w"], nloads[0])
            c = [0]

            def link(ins):
                c[0] += 1
                ins.then_inc(s_c["prep"], 1)
                v.wait_ge(s_c["prep"], c[0])
            link(v.tensor_scalar(onepe[:, :], onepe[:, :], 1.0, None, ALU.add))
            link(v.tensor_copy(dF, dI))
            link(v.tensor_copy(dnF, dnI))
            link(v.memset(NEG[:, 0:1], -BIG))
            link(v.tensor_tensor(out=NEG[:, 1:C], in0=dF[:, 1:C], in1=dF[:, 0:C - 1], op=ALU.not_equal))
            link(v.tensor_scalar(NEG[:, 1:C], NEG[:, 1:C], -BIG, None, ALU.mult))
            link(v.tensor_copy(IDX[:, 0, :], sS))
            link(v.tensor_scalar(IDX[:, 1, :], dF, float(N - 1), None, ALU.min))
            link(v.tensor_tensor(out=lastF, in0=dF, in1=dnF, op=ALU.not_equal))
            link(v.scalar_tensor_tensor(out=dnF, in0=dF, scalar=trash[:, 0:1], in1=lastF, op0=ALU.subtract, op1=ALU.mult))
            link(v.tensor_scalar(IDX[:, 2, :], dnF, trash[:, 0:1], None, ALU.add))
            v.wait_ge(q["row"], 1)
            link(v.tensor_scalar(CT[:, :], psum[:, 7, 0:P], dF[:, 0:1], None, ALU.is_equal))
            link(v.tensor_tensor(out=CT[:, :], in0=CT[:, :], in1=lower[:, :], op=ALU.mult))
            link(v.tensor_reduce(cnt[:, 0:1], CT[:, :], AXX, ALU.max))
            link(v.tensor_scalar(CT[:, :], CT[:, :], -1.0, BIG, ALU.add, ALU.mult))
            link(v.tensor_tensor(out=cnt[:, 1:2], in0=dF[:, 0:1], in1=dF[:, C - 1:C], op=ALU.not_equal))
            link(v.tensor_tensor(out=cnt[:, 1:2], in0=cnt[:, 1:2], in1=lastF[:, C - 1:C], op=ALU.max))
            link(v.tensor_tensor(out=cnt[:, 2:3], in0=cnt[:, 0:1], in1=cnt[:, 1:2], op=ALU.mult))
            link(v.scalar_tensor_tensor(out=cnt[:, 3:4], in0=dF[:, 0:1], scalar=trash[:, 0:1], in1=cnt[:, 2:3], op0=ALU.subtract, op1=ALU.mult))
            link(v.tensor_scalar(fixs[:, :], cnt[:, 3:4], trash[:, 0:1], None, ALU.add))
            link(v.tensor_scalar(fixg[:, :], dF[:, 0:1], float(N - 1), None, ALU.min))
            v.wait_ge(s_c["wg3"], FH)
            for L, H in ((2, H2), (3, H3)):
                for i in range(2):
                    for f in range(FH):
                        link(v.tensor_tensor(out=mulA[:, f, :], in0=Wg[L][:, f, 0:D], in1=att[L][:, i, :], op=ALU.mult))
                    for f in range(FH):
                        link(v.tensor_reduce(Wg[L][:, f, D + i * H:D + (i + 1) * H],
                                             mulA[:, f, :].rearrange("p (h d) -> p h d", h=H), AXX, ALU.add))

            def indices(k):
                wait(v, e1_xg[k.b], 16 * J * k.n)
                v.tensor_scalar(gidx[:, k.b, :], dstI[:, k.s, :], 0.0, None, ALU.add).then_inc(q["gix"], 1)

            def first(k):
                wait(v, q["csum"], J * (k.s - 1))
                v.tensor_scalar(srcF[:, k.b, :], srcI[:, k.s, :], 0.0, None, ALU.add).then_inc(q["srcF"], 1)

            indices(at(0))

            def body(k):
                if live(k.plus(1), ES):
                    indices(k.plus(1))
                first(k)
                v.wait_ge(q["srow"], k.s + 1)
                for j in range(J):
                    v.tensor_scalar(same[:, k.b, j, :], psum[:, k.b, j * P:(j + 1) * P], srcF[:, k.b, j:j + 1], None,
                                    ALU.is_equal).then_inc(q["same"], 1)
                for j in range(J):
                    v.wait_ge(q["same"], J * k.s + j + 1)
                    v.tensor_tensor_reduce(out=junk[:, j, :], in0=same[:, k.b, j, :], in1=lower[:, :], scale=1.0, scalar=0.0,
                                           op0=ALU.mult, op1=ALU.add, accum_out=cnt[:, j:j + 1]).then_inc(q["cnt"], 1)
                v.wait_ge(q["cnt"], J * (k.s + 1))
                v.tensor_scalar(fst, cnt, 0.5, None, ALU.is_lt).then_inc(q["first"], 1)
                v.wait_ge(q["first"], k.s + 1)
                v.scalar_tensor_tensor(out=fsd, in0=srcF[:, k.b, :], scalar=trash[:, 0:1], in1=fst,
                                       op0=ALU.subtract, op1=ALU.mult).then_inc(q["d"], 1)
                v.wait_ge(q["d"], k.s + 1)
                wait(v, q["scat"], 16 * J * (k.s - 1))
                v.tensor_scalar(sidx[:, k.b, :], fsd, trash[:, 0:1], None, ALU.add).then_inc(q["sidx"], 1)
                v.wait_ge(e1_xg[k.b], 16 * J * (k.n + 1))
                v.wait_ge(e1_ea[k.b], 32 * (k.n + 1))
                v.tensor_tensor(out=msg[:, k.b, :, 0:D], in0=xg[:, k.b, :, :], in1=eat[:, k.b, :, :], op=ALU.mult).then_inc(q["msg"], 1)
            run_steps(v, ES, body)

        def p1_tensor(pe):
            pe.wait_ge(s_c["id"], 8)
            pe.wait_ge(s_c["w"], nloads[0])
            for f in range(FH):
                for g in range(FH):
                    last = pe.transpose(psum[:, 4 + f, g * P:(g + 1) * P], lda[:, g, f * P:(f + 1) * P], ident[:, :])
                last.then_inc(q["wt"], 1)
            for k in range(KH):
                pe.matmul(psum[:, 6, k:k + 1], W1u[:, k * P:(k + 1) * P], u0[:, :], start=True, stop=True).then_inc(q["wt"], 1)
            pe.wait_ge(s_c["prep"], 3)
            pe.matmul(psum[:, 7, 0:P], dF[:, C - 1:C].to_broadcast([P, P]), ident[:, :], start=True, stop=True).then_inc(q["row"], 1)

            def rows(k):
                pe.wait_ge(q["srcF"], k.s + 1)
                for j in range(J):
                    last = pe.matmul(psum[:, k.b, j * P:(j + 1) * P], srcF[:, k.b, j:j + 1].to_broadcast([P, P]), ident[:, :],
                                     start=True, stop=True)
                last.then_inc(q["srow"], 1)

            def body(k):
                rows(k)
                pe.wait_ge(q["msg"], k.s + 1)
                for j in range(J):
                    wait(pe, q["comb"], J * k.s + j - 1)
                    pe.matmul(psum[:, 2 + j % 2, 0:TW0], same[:, k.b, j, :], msg[:, k.b, j, :], start=True, stop=True).then_inc(q["csum"], 1)
            run_steps(pe, ES, body)

        fresh()
        p2x = take([2, J, D])
        p2a = take([2, J, D])
        p2h = take([2, J, D])
        hT = take([2, FH, STEP])
        h1 = take([2, FH, STEP])
        st = take([FH, NS, 6])
        mvb = take([FH, 2])
        tA = take([FH, 1])
        p2 = {k: sem(f"p2_{k}") for k in ("h", "tr", "hT", "mm", "h1", "st", "fin", "sq")}
        p2_x = [sem(f"p2_x{b}") for b in range(2)]
        p2_a = [sem(f"p2_a{b}") for b in range(2)]
        p2_w = [sem(f"p2_w{b}") for b in range(2)]

        def p2_sync(sp):
            r = p2

            def store(k):
                sp.wait_ge(r["h1"], FH * (k.s + 1))
                sp.dma_start(h1_d[k.s, :, :, :], h1[:, k.b, :, :]).then_inc(p2_w[k.b], 16)

            def body(k):
                wait(sp, r["h"], k.s - 1)
                a, n = node_view(x, k)
                sp.dma_start(p2x[0:n, k.b, :, :], a).then_inc(p2_x[k.b], 16)
                a, n = node_view(tab0, k, slice(0, D))
                sp.dma_start(p2a[0:n, k.b, :, :], a).then_inc(p2_a[k.b], 16)
                if not (k.known() and k.s < 3):
                    store(k.plus(-3))
            run_steps(sp, NS, body, peel=4)
            for s in (NS - 3, NS - 2, NS - 1):
                store(at(s))
            for b in range(2):
                sp.wait_ge(p2_w[b], 16 * ((NS + 1 - b) // 2))

        def p2_vector(v):
            r = p2

            def h(k):
                v.wait_ge(p2_x[k.b], 16 * (k.n + 1))
                v.wait_ge(p2_a[k.b], 16 * (k.n + 1))
                wait(v, r["tr"], k.s - 1)
                v.scalar_tensor_tensor(out=p2h[:, k.b, :, :], in0=p2x[:, k.b, :, :], scalar=onepe[:, 0:1], in1=p2a[:, k.b, :, :],
                                       op0=ALU.mult, op1=ALU.add).then_inc(r["h"], 1)

            h(Step(0, 0, 0))

            def body(k):
                nxt = k.plus(1)
                if not (nxt.known() and nxt.s >= NS):
                    h(nxt)
                for g in range(FH):
                    v.wait_ge(r["h1"], FH * k.s + g + 1)
                    a = h1[:, k.b, g, :]
                    if k.known() and k.s == NS - 1:
                        a = a.rearrange("p (j q) -> p j q", j=J)[:, :, 0:NLAST]
                    v.wait_ge(s_c["id"], 8)
                    v.bn_stats(st[:, g, k.s, :], a).then_inc(r["st"], 1)
            run_steps(v, NS, body)
            v.wait_ge(r["st"], FH * NS)
            for g in range(FH):
                v.bn_aggr(mvb[:, g, :], st[:, g, :, :].rearrange("p s c -> p (s c)")).then_inc(r["fin"], 1)
            v.wait_ge(r["fin"], FH)
            v.tensor_scalar(tA, mvb[:, :, 1:2], LN_EPS, None, ALU.add).then_inc(r["fin"], 1)
            v.wait_ge(r["sq"], 1)
            v.tensor_tensor(out=bnA[:, :], in0=tA[:, :, 0], in1=colv[:, 1, :], op=ALU.mult).then_inc(r["fin"], 1)
            v.wait_ge(r["fin"], FH + 2)
            v.tensor_tensor(out=bnB[:, :], in0=mvb[:, :, 0], in1=bnA[:, :], op=ALU.mult).then_inc(r["fin"], 1)
            v.wait_ge(r["fin"], FH + 3)
            v.tensor_tensor(out=bnB[:, :], in0=colv[:, 2, :], in1=bnB[:, :], op=ALU.subtract).then_inc(r["fin"], 1)

        def p2_gpsimd(pool):
            pool.wait_ge(p2["fin"], FH + 1)
            pool.tensor_tensor(out=tA[:, :, 0], in0=tA[:, :, 0], in1=expo[:, 0:FH], op=ALU.pow).then_inc(p2["sq"], 1)

        def p2_scalar(act):
            r = p2

            def evac(k):
                act.wait_ge(r["tr"], k.s + 1)
                wait(act, r["mm"], FH * (k.s - 1))
                for f in range(FH):
                    act.activation(hT[:, k.b, f, :], psum[:, 2 * k.b + f, :], ACT.Copy).then_inc(r["hT"], 1)

            evac(Step(0, 0, 0))

            def body(k):
                nxt = k.plus(1)
                if not (nxt.known() and nxt.s >= NS):
                    evac(nxt)
                wait(act, p2_w[k.b], 16 * k.n)
                wait(act, r["st"], FH * (k.s - 1))
                for g in range(FH):
                    act.wait_ge(r["mm"], FH * k.s + g + 1)
                    act.activation(h1[:, k.b, g, :], psum[:, 4 + 2 * k.b + g, :], ACT.Identity, bias=colv[:, 0, g:g + 1]).then_inc(r["h1"], 1)
            run_steps(act, NS, body)

        def p2_tensor(pe):
            r = p2

            def tr(k):
                pe.wait_ge(r["h"], k.s + 1)
                wait(pe, r["hT"], FH * (k.s - 1))
                for f in range(FH):
                    for j in range(J):
                        last = pe.transpose(psum[:, 2 * k.b + f, j * P:(j + 1) * P], p2h[:, k.b, j, f * P:(f + 1) * P], ident[:, :])
                last.then_inc(r["tr"], 1)

            tr(Step(0, 0, 0))

            def body(k):
                nxt = k.plus(1)
                if not (nxt.known() and nxt.s >= NS):
                    tr(nxt)
                pe.wait_ge(r["hT"], FH * (k.s + 1))
                wait(pe, r["h1"], FH * (k.s - 1))
                for g in range(FH):
                    for f in range(FH):
                        last = pe.matmul(psum[:, 4 + 2 * k.b + g, :], W1a[:, f, g * P:(g + 1) * P], hT[:, k.b, f, :],
                                         start=(f == 0), stop=(f == FH - 1))
                    last.then_inc(r["mm"], 1)
            run_steps(pe, NS, body)

        def linker(eng, sm, k, per_step):
            c = [0]

            def link(ins):
                c[0] += 1
                assert c[0] <= per_step
                ins.then_inc(sm, 1)
                eng.wait_ge(sm, k.s * per_step + c[0])
            return link

        class Norm:
            def __init__(self, sems):
                self.st = take([J, 6])
                self.mv = take([J, 2])
                self.ve = take([J])
                self.rs = take([J])
                self.hold = take([1])
                self.s = sems

            def stats(self, v, k, r):
                for j in range(J):
                    v.bn_stats(self.st[:, j, :], r[:, j, :]).then_inc(self.s["st"], 1)
                wait(v, self.s["ve"], k.s)
                v.wait_ge(self.s["st"], J * (k.s + 1))
                v.memset(self.hold, 0.0)
                for j in range(J):
                    v.bn_aggr(self.mv[:, j, :], self.st[:, j, :]).then_inc(self.s["mv"], 1)

            def rstd(self, pool, k):
                pool.wait_ge(self.s["mv"], J * (k.s + 1))
                pool.tensor_tensor(out=self.ve, in0=self.mv[:, :, 1], in1=lneps[:, :], op=ALU.add).then_inc(self.s["ve"], 1)
                wait(pool, self.s["y"], J * k.s)
                pool.wait_ge(self.s["ve"], k.s + 1)
                pool.tensor_tensor(out=self.rs, in0=self.ve, in1=expo[:, :], op=ALU.pow).then_inc(self.s["rs"], 1)

            def scale(self, v, k, r, y):
                v.wait_ge(self.s["rs"], k.s + 1)
                for j in range(J):
                    v.tensor_scalar(y[:, j, :], r[:, j, :], self.mv[:, j, 0:1], self.rs[:, j:j + 1],
                                    ALU.subtract, ALU.mult).then_inc(self.s["y"], 1)

        fresh()
        p3h = take([2, FH, STEP])
        p3y = take([FH, STEP])
        p3x = take([2, J, D])
        p3e = take([2, J, DE + 4])
        em = take([J, DE])
        rc = take([J])
        rA = take([J, D])
        x1 = take([2, J, D])
        x1b = take([2, J, D])
        x1T = take([FH, STEP])
        eT = take([STEP], parts=DE)
        hid = take([KH, STEP])
        x2 = take([2, J, D])
        lnA = Norm({k: sem(f"lnA_{k}") for k in ("st", "mv", "ve", "rs", "y")})
        lnB = Norm({k: sem(f"lnB_{k}") for k in ("st", "mv", "ve", "rs", "y")})
        p3 = {k: sem(f"p3_{k}") for k in ("y", "xb", "mmA", "rA", "mx", "rc", "em", "ringw", "ringr", "trx", "x1T",
                                          "x1b", "mmB", "rB")}
        p3_h = [sem(f"p3_h{b}") for b in range(2)]
        p3_x = [sem(f"p3_x{b}") for b in range(2)]
        p3_e = [sem(f"p3_e{b}") for b in range(2)]
        p3_w = [sem(f"p3_w{b}") for b in range(2)]
        BA, BT, BR, BB = 0, 2, 4, 6

        def outA(j):
            return psum[:, BA + j // 2, (j % 2) * D:(j % 2 + 1) * D]

        def outB(j):
            return psum[:, BB + j // 2, (j % 2) * D:(j % 2 + 1) * D]

        def p3_sync(sp):
            def store(k):
                sp.wait_ge(lnB.s["y"], J * (k.s + 1))
                a, n = node_view(x2_d, k)
                sp.dma_start(a, x2[0:n, k.b, :, :]).then_inc(p3_w[k.b], 16)

            def body(k):
                wait(sp, p3["y"], FH * (k.s - 1))
                sp.dma_start(p3h[:, k.b, :, :], h1_d[k.s, :, :, :]).then_inc(p3_h[k.b], 16)
                wait(sp, p3["rA"], 2 * (k.s - 1))
                a, n = node_view(x, k)
                sp.dma_start(p3x[0:n, k.b, :, :], a).then_inc(p3_x[k.b], 16)
                wait(sp, p3["em"], k.s - 1)
                a, n = node_view(tab0, k, slice(D, TW0))
                sp.dma_start(p3e[0:n, k.b, :, :], a).then_inc(p3_e[k.b], 16)
                if not (k.known() and k.s < 3):
                    store(k.plus(-3))
            run_steps(sp, NS, body, peel=4)
            for s in (NS - 3, NS - 2, NS - 1):
                store(Step(s, s % 2, s // 2))
            for b in range(2):
                sp.wait_ge(p3_w[b], 16 * ((NS + 1 - b) // 2))

        def p3_gpsimd(pool):
            def xb(k):
                pool.wait_ge(p3_x[k.b], 16 * (k.n + 1))
                pool.tensor_tensor(out=p3x[:, k.b, :, :], in0=p3x[:, k.b, :, :],
                                   in1=b2a[:, :].rearrange("p (a d) -> p a d", a=1).to_broadcast([P, J, D]), op=ALU.add).then_inc(p3["xb"], 1)

            def x1_b(k):
                pool.wait_ge(lnA.s["y"], J * (k.s + 1))
                wait(pool, p3["rB"], 2 * (k.s - 1))
                pool.tensor_tensor(out=x1b[:, k.b, :, :], in0=x1[:, k.b, :, :],
                                   in1=b2b[:, :].rearrange("p (a d) -> p a d", a=1).to_broadcast([P, J, D]), op=ALU.add).then_inc(p3["x1b"], 1)
            k0 = Step(0, 0, 0)
            xb(k0)
            lnA.rstd(pool, k0)
            x1_b(k0)

            def body(k):
                nxt = k.plus(1)
                if live(nxt, NS):
                    xb(nxt)
                    lnA.rstd(pool, nxt)
                    x1_b(nxt)
                lnB.rstd(pool, k)
            run_steps(pool, NS, body)

        def p3_scalar(act):
            def y(k):
                act.wait_ge(p3_h[k.b], 16 * (k.n + 1))
                wait(act, p3["mmA"], J * k.s)
                for f in range(FH):
                    act.activation(p3y[:, f, :], p3h[:, k.b, f, :], ACT.Relu, bias=bnB[:, f:f + 1], scale=bnA[:, f:f + 1]).then_inc(p3["y"], 1)

            def evac(k):
                act.wait_ge(p3["ringw"], 5 * k.s + 1)
                wait(act, p3["mmB"], J * (k.s - 1))
                act.activation(eT, psum[0:DE, BR + k.b, :], ACT.Copy).then_inc(p3["ringr"], 1)
                act.wait_ge(p3["trx"], k.s + 1)
                for f in range(FH):
                    act.activation(x1T[:, f, :], psum[:, BT + f, :], ACT.Copy).then_inc(p3["x1T"], 1)

            def relu(k):
                wait(act, p3["mmB"], J * k.s)
                for c in range(KH):
                    act.wait_ge(p3["ringw"], 5 * k.s + 2 + c)
                    act.activation(hid[:, c, :], psum[:, BR + (k.b + 1 + c) % 2, :], ACT.Relu, bias=hbias[:, c:c + 1]).then_inc(p3["ringr"], 1)
            k0 = Step(0, 0, 0)
            y(k0)
            evac(k0)
            y(k0.plus(1))

            def body(k):
                relu(k)
                if live(k.plus(1), NS):
                    evac(k.plus(1))
                if live(k.plus(2), NS):
                    y(k.plus(2))
            run_steps(act, NS, body)

        def p3_vector(v):
            def first(k):
                v.wait_ge(p3_e[k.b], 16 * (k.n + 1))
                v.tensor_scalar(rc, p3e[:, k.b, :, DE], 1.0, None, ALU.max).then_inc(p3["mx"], 1)
                v.wait_ge(p3["mx"], k.s + 1)
                v.reciprocal(rc, rc).then_inc(p3["rc"], 1)
                v.wait_ge(p3["rc"], k.s + 1)
                wait(v, p3["ringw"], 5 * (k.s - 1) + 1)
                v.tensor_tensor(out=em, in0=p3e[:, k.b, :, 0:DE],
                                in1=rc.rearrange("p (j a) -> p j a", a=1).to_broadcast([P, J, DE]), op=ALU.mult).then_inc(p3["em"], 1)
                v.wait_ge(p3["xb"], k.s + 1)
                for i in range(2):
                    v.wait_ge(p3["mmA"], J * k.s + 2 * i + 2)
                    v.tensor_tensor(out=rA[:, 2 * i:2 * i + 2, :], in0=psum[:, BA + i, :].rearrange("p (j d) -> p j d", j=2),
                                    in1=p3x[:, k.b, 2 * i:2 * i + 2, :], op=ALU.add).then_inc(p3["rA"], 1)
                v.wait_ge(p3["rA"], 2 * (k.s + 1))
                lnA.stats(v, k, rA)
                wait(v, p3["x1b"], k.s - 1)
                wait(v, p3["trx"], k.s - 1)
                lnA.scale(v, k, rA, x1[:, k.b, :, :])

            def second(k):
                v.wait_ge(p3["x1b"], k.s + 1)
                wait(v, p3_w[k.b], 16 * k.n)
                for i in range(2):
                    v.wait_ge(p3["mmB"], J * k.s + 2 * i + 2)
                    v.tensor_tensor(out=x1b[:, k.b, 2 * i:2 * i + 2, :], in0=psum[:, BB + i, :].rearrange("p (j d) -> p j d", j=2),
                                    in1=x1b[:, k.b, 2 * i:2 * i + 2, :], op=ALU.add).then_inc(p3["rB"], 1)
                v.wait_ge(p3["rB"], 2 * (k.s + 1))
                lnB.stats(v, k, x1b[:, k.b, :, :])
                lnB.scale(v, k, x1b[:, k.b, :, :], x2[:, k.b, :, :])
            first(Step(0, 0, 0))

            def body(k):
                if live(k.plus(1), NS):
                    first(k.plus(1))
                second(k)
            run_steps(v, NS, body)

        def p3_tensor(pe):
            def mmA(k):
                pe.wait_ge(p3["y"], FH * (k.s + 1))
                wait(pe, p3["rA"], 2 * k.s)
                for j in range(J):
                    for f in range(FH):
                        last = pe.matmul(outA(j), p3y[:, f, j * P:(j + 1) * P], W2a[:, f, :], start=(f == 0), stop=(f == FH - 1))
                    last.then_inc(p3["mmA"], 1)

            def tr(k):
                pe.wait_ge(p3["em"], k.s + 1)
                wait(pe, p3["x1T"], FH * k.s)
                wait(pe, p3["ringr"], 5 * k.s - 1)
                pe.wait_ge(lnA.s["y"], J * (k.s + 1))
                for f in range(FH):
                    for j in range(J):
                        last = pe.transpose(psum[:, BT + f, j * P:(j + 1) * P], x1[:, k.b, j, f * P:(f + 1) * P], ident[:, :])
                last.then_inc(p3["trx"], 1)
                for j in range(J):
                    last = pe.transpose(psum[0:DE, BR + k.b, j * P:(j + 1) * P], em[:, j, :], ident[:, :])
                last.then_inc(p3["ringw"], 1)

            def hidden(k):
                pe.wait_ge(p3["x1T"], FH * (k.s + 1))
                for c in range(KH):
                    pe.wait_ge(p3["ringr"], 5 * k.s + max(c, 1))
                    o = psum[:, BR + (k.b + 1 + c) % 2, :]
                    pe.matmul(o, W1b[:, 0, c * P:(c + 1) * P], x1T[:, 0, :], start=True, stop=False)
                    pe.matmul(o, W1b[:, 1, c * P:(c + 1) * P], x1T[:, 1, :], start=False, stop=False)
                    pe.matmul(o, W1e[:, c * P:(c + 1) * P], eT, start=False, stop=True).then_inc(p3["ringw"], 1)

            def mmB(k):
                wait(pe, p3["rB"], 2 * k.s)
                pe.wait_ge(p3["ringr"], 5 * (k.s + 1))
                for j in range(J):
                    for c in range(KH):
                        last = pe.matmul(outB(j), hid[:, c, j * P:(j + 1) * P], W2b[:, c, :], start=(c == 0), stop=(c == KH - 1))
                    last.then_inc(p3["mmB"], 1)
            k0 = Step(0, 0, 0)
            mmA(k0)
            tr(k0)

            def body(k):
                nxt = k.plus(1)
                if live(nxt, NS):
                    mmA(nxt)
                hidden(k)
                if live(nxt, NS):
                    tr(nxt)
                mmB(k)
            run_steps(pe, NS, body)

        PHASES.append((p1_sync, p1_scalar, p1_gpsimd, p1_vector, p1_tensor))
        PHASES.append((p2_sync, p2_scalar, p2_gpsimd, p2_vector, p2_tensor))
        PHASES.append((p3_sync, p3_scalar, p3_gpsimd, p3_vector, p3_tensor))

        once = {k: sem(f"g_{k}") for k in ("zero", "end", "old", "mb", "zb", "mx", "mt", "z2", "wx", "f0", "tw", "wT", "car", "new", "fr", "fix")}
        edge2 = {k: sem(f"g_{k}") for k in
                 ("gix", "six", "tr", "ev", "mm", "eL", "e", "q", "M", "d", "w", "sA", "s", "A", "B", "S")}
        gs = [sem(f"g_g{b}") for b in range(2)]
        sc = [sem(f"g_s{b}") for b in range(2)]

        def edge_pass(L, xtab, H):
            fresh()
            HD = D // H
            gix = take([2, 2, J], I32)
            six = take([2, J], I32)
            xs = take([2, J, D])
            xd = take([2, J, D])
            xT = take([2, 4, P])
            row = take([2, J, TW])
            eL = take([J, H])
            ee = take([J, H])
            qq = take([J, H])
            dd = take([2, J, H])
            ww = take([2, 2, J, H])
            tS = take([J, H])
            tB = take([2, D])
            endrow = take([TW])
            oldrow = take([TW])
            newrow = take([TW])
            zb = take([H, P])
            wT = take([H, P])
            mx = take([H])
            mt = take([H])
            f0 = take([H])
            r = dict(edge2, **once)
            T = L - 1
            S0 = (L - 2) * CS
            S1 = S0 + CS
            F0 = 2

            def g_sync(sp):
                pass

            def g_gpsimd(pool):
                pool.memset(row, 0.0).then_inc(r["zero"], 1)
                pool.wait_ge(s_c["fill1"], 16 * NFILL)

                def gather(k):
                    wait(pool, r["tr"], J * (k.s - 1))
                    pool.wait_ge(r["gix"], k.s + 1)
                    settle(pool, 2, k.s)
                    for j in range(J):
                        for n, o in ((0, xs), (1, xd)):
                            pool.indirect_dma_start(out=o[:, k.b, j, :], out_offset=None, in_=xtab[:, :],
                                                    in_offset=bass.IndirectOffsetOnAxis(ap=gix[:, k.b, n, j:j + 1], axis=0)).then_inc(gs[k.b], 16)

                def scatter(k):
                    pool.wait_ge(r["S"], J * (k.s + 1))
                    pool.wait_ge(r["six"], k.s + 1)
                    settle(pool, 3, k.s)
                    for j in range(J):
                        pool.indirect_dma_start(out=tab[:, :], out_offset=bass.IndirectOffsetOnAxis(ap=six[:, k.b, j:j + 1], axis=0),
                                                in_=row[:, k.b, j, :], in_offset=None, bounds_check=N - 1, oob_is_err=False).then_inc(sc[k.b], 16)
                gather(at(S0))

                def body(k):
                    if live(k.plus(1), S1):
                        gather(k.plus(1))
                    if not (k.known() and k.s == S0):
                        scatter(k.plus(-1))
                run_steps(pool, CS, body, S0)
                scatter(at(S1 - 1))
                for b in range(2):
                    pool.wait_ge(sc[b], 16 * J * ((S1 + 1 - b) // 2))
                pool.indirect_dma_start(out=oldrow[:, :], out_offset=None, in_=tab[:, :],
                                        in_offset=bass.IndirectOffsetOnAxis(ap=fixg[:, 0:1], axis=0)).then_inc(r["old"], 16)
                pool.wait_ge(r["fr"], 3 * T)
                pool.wait_ge(r["new"], 3 * T)
                pool.indirect_dma_start(out=tab[:, :], out_offset=bass.IndirectOffsetOnAxis(ap=fixs[:, 0:1], axis=0),
                                        in_=newrow[:, :], in_offset=None, bounds_check=N - 1, oob_is_err=False).then_inc(r["fix"], 16)
                pool.wait_ge(r["fix"], 16 * T)

            def g_tensor(pe):
                def tr(k, j):
                    if j == 0:
                        pe.wait_ge(gs[k.b], 16 * 2 * J * (k.n + 1))
                    wait(pe, r["ev"], J * k.s + j - 1)
                    for i, a in enumerate((xs, xd)):
                        for f in range(FH):
                            last = pe.transpose(psum[:, j % 2, (2 * i + f) * P:(2 * i + f + 1) * P], a[:, k.b, j, f * P:(f + 1) * P], ident[:, :])
                    last.then_inc(r["tr"], 1)

                def mm(k, j):
                    pe.wait_ge(r["ev"], J * k.s + j + 1)
                    wait(pe, r["B"], J * (k.s - 1) + j + 1)
                    wait(pe, r["e"], k.s)
                    o = psum[:, F0 + j, :]
                    for f in range(FH):
                        pe.matmul(o[:, 0:D + H], xT[:, j % 2, f, :], Wg[L][:, f, 0:D + H], start=(f == 0), stop=False)
                    for f in range(FH):
                        last = pe.matmul(o[:, D:D + H], xT[:, j % 2, 2 + f, :], Wg[L][:, f, D + H:D + 2 * H], start=False, stop=(f == FH - 1))
                    last.then_inc(r["mm"], 1)
                tr(at(S0), 0)

                def body(k):
                    for j in range(J):
                        if j + 1 < J:
                            tr(k, j + 1)
                        elif live(k.plus(1), S1):
                            tr(k.plus(1), 0)
                        mm(k, j)
                run_steps(pe, CS, body, S0)
                pe.wait_ge(r["end"], T)
                for h in range(H):
                    last = pe.matmul(psum[:, h // 4, (h % 4) * P:(h % 4 + 1) * P], endrow[:, MC + h:MC + h + 1].to_broadcast([P, P]), ident[:, :],
                                     start=True, stop=True)
                last.then_inc(r["mb"], 1)
                pe.wait_ge(r["wx"], T)
                for h in range(H):
                    last = pe.transpose(psum[:, F0 + h // 4, (h % 4) * P:(h % 4 + 1) * P], zb[:, h, :], ident[:, :])
                last.then_inc(r["tw"], 1)
                pe.wait_ge(r["wT"], T)
                for h in range(H):
                    pe.matmul(psum[:, F0 + 2, h * HD:(h + 1) * HD], wT[:, h, :], endrow[:, h * HD:(h + 1) * HD], start=True, stop=True)
                for h in range(H):
                    last = pe.matmul(psum[:, F0 + 3, h:h + 1], wT[:, h, :], endrow[:, SC + h:SC + h + 1], start=True, stop=True)
                last.then_inc(r["car"], 1)

            def g_scalar(act):
                def ev(k, j):
                    act.wait_ge(r["tr"], J * k.s + j + 1)
                    wait(act, r["mm"], J * k.s + j - 1)
                    act.activation(xT[:, j % 2, :, :], psum[:, j % 2, :].rearrange("p (i n) -> p i n", n=P), ACT.Copy).then_inc(r["ev"], 1)

                def ex(k):
                    act.wait_ge(r["d"], 2 * (k.s + 1))
                    wait(act, r["S"], J * (k.s - 1))
                    act.activation(ww[:, k.b, :, :, :], dd, ACT.Exp).then_inc(r["w"], 1)

                def body(k):
                    for j in range(J):
                        ev(k, j)
                    ex(k)
                ev(at(S0), 0)

                def body(k):
                    for j in range(1, J):
                        ev(k, j)
                    if live(k.plus(1), S1):
                        ev(k.plus(1), 0)
                    ex(k)
                run_steps(act, CS, body, S0)
                act.wait_ge(r["z2"], 2 * T)
                act.activation(zb, zb, ACT.Exp).then_inc(r["wx"], 1)
                act.activation(f0, mx, ACT.Exp).then_inc(r["f0"], 1)
                act.wait_ge(r["tw"], T)
                act.activation(wT, psum[:, F0:F0 + H // 4, :].rearrange("p a (h n) -> p (a h) n", n=P), ACT.Copy).then_inc(r["wT"], 1)

            def heads(a):
                return a.rearrange("p (h a) -> p h a", a=1).to_broadcast([P, H, HD])

            def g_vector(v):
                v.wait_ge(r["zero"], T)

                def indices(k):
                    wait(v, gs[k.b], 16 * 2 * J * k.n)
                    v.tensor_scalar(gix[:, k.b, :, :], IDX[:, 0:2, bass.ds((k.s - S0) * J, J)], 0.0, None, ALU.add).then_inc(r["gix"], 1)
                indices(at(S0))

                def body(k):
                    if live(k.plus(1), S1):
                        indices(k.plus(1))
                    b = k.b
                    prev = lambda j, lo, hi: row[:, b, j - 1, lo:hi] if j else row[:, 1 - b, J - 1, lo:hi]
                    scores = psum[:, F0:F0 + J, D:D + H]
                    v.wait_ge(r["mm"], J * (k.s + 1))
                    v.tensor_scalar(eL, scores, SLOPE, None, ALU.mult).then_inc(r["eL"], 1)
                    v.wait_ge(r["eL"], k.s + 1)
                    v.tensor_tensor(out=ee, in0=scores, in1=eL, op=ALU.max).then_inc(r["e"], 1)
                    v.wait_ge(r["e"], k.s + 1)
                    wait(v, sc[b], 16 * J * k.n)
                    v.tensor_scalar(six[:, b, :], IDX[:, 2, bass.ds((k.s - S0) * J, J)], 0.0, None, ALU.add).then_inc(r["six"], 1)
                    for j in range(J):
                        wait(v, r["M"], J * k.s + j)
                        v.tensor_scalar(qq[:, j, :], prev(j, MC, MC + H), NEG[:, bass.ds((k.s - S0) * J + j, 1)], None, ALU.add).then_inc(r["q"], 1)
                        v.wait_ge(r["q"], J * k.s + j + 1)
                        v.tensor_tensor(out=row[:, b, j, MC:MC + H], in0=qq[:, j, :], in1=ee[:, j, :], op=ALU.max).then_inc(r["M"], 1)
                    v.wait_ge(r["M"], J * (k.s + 1))
                    wait(v, r["w"], k.s)
                    v.tensor_tensor(out=dd[:, 0, :, :], in0=qq, in1=row[:, b, :, MC:MC + H], op=ALU.subtract).then_inc(r["d"], 1)
                    v.tensor_tensor(out=dd[:, 1, :, :], in0=ee, in1=row[:, b, :, MC:MC + H], op=ALU.subtract).then_inc(r["d"], 1)
                    v.wait_ge(r["w"], k.s + 1)
                    for j in range(J):
                        wait(v, r["s"], J * k.s + j)
                        v.tensor_tensor(out=tS[:, j, :], in0=prev(j, SC, SC + H), in1=ww[:, b, 0, j, :], op=ALU.mult).then_inc(r["sA"], 1)
                        v.wait_ge(r["sA"], J * k.s + j + 1)
                        v.tensor_tensor(out=row[:, b, j, SC:SC + H], in0=tS[:, j, :], in1=ww[:, b, 1, j, :], op=ALU.add).then_inc(r["s"], 1)
                    for j in range(J):
                        wait(v, r["S"], J * k.s + j)
                        v.tensor_tensor(out=row[:, b, j, 0:D].rearrange("p (h c) -> p h c", h=H),
                                        in0=prev(j, 0, D).rearrange("p (h c) -> p h c", h=H), in1=heads(ww[:, b, 0, j, :]), op=ALU.mult).then_inc(r["A"], 1)
                        v.tensor_tensor(out=tB[:, j % 2, :].rearrange("p (h c) -> p h c", h=H),
                                        in0=psum[:, F0 + j, 0:D].rearrange("p (h c) -> p h c", h=H), in1=heads(ww[:, b, 1, j, :]), op=ALU.mult).then_inc(r["B"], 1)
                        v.wait_ge(r["A"], J * k.s + j + 1)
                        v.wait_ge(r["B"], J * k.s + j + 1)
                        v.tensor_tensor(out=row[:, b, j, 0:D], in0=row[:, b, j, 0:D], in1=tB[:, j % 2, :], op=ALU.add).then_inc(r["S"], 1)
                run_steps(v, CS, body, S0)
                v.wait_ge(r["S"], J * S1)
                v.wait_ge(r["s"], J * S1)
                v.tensor_copy(endrow, row[:, (S1 - 1) % 2, J - 1, :]).then_inc(r["end"], 1)
                v.wait_ge(r["mb"], T)
                v.tensor_tensor(out=zb, in0=psum[:, 0:H // 4, :].rearrange("p a (h n) -> p (a h) n", n=P),
                                in1=CT[:, :].rearrange("p (a n) -> p a n", a=1).to_broadcast([P, H, P]), op=ALU.add).then_inc(r["zb"], 1)
                v.wait_ge(r["zb"], T)
                v.tensor_reduce(mx, zb, AXX, ALU.max).then_inc(r["mx"], 1)
                v.wait_ge(r["mx"], T)
                v.wait_ge(r["old"], 16 * T)
                v.tensor_tensor(out=mt, in0=mx, in1=oldrow[:, MC:MC + H], op=ALU.max).then_inc(r["mt"], 1)
                v.wait_ge(r["mt"], T)
                v.tensor_tensor(out=zb, in0=zb, in1=mt.rearrange("p (h a) -> p h a", a=1).to_broadcast([P, H, P]), op=ALU.subtract).then_inc(r["z2"], 1)
                v.tensor_tensor(out=mx, in0=oldrow[:, MC:MC + H], in1=mt, op=ALU.subtract).then_inc(r["z2"], 1)
                v.wait_ge(r["f0"], T)
                v.tensor_copy(newrow, endrow).then_inc(r["fr"], 1)
                v.wait_ge(r["fr"], 3 * T - 2)
                v.tensor_copy(newrow[:, MC:MC + H], mt).then_inc(r["new"], 1)
                v.tensor_tensor(out=newrow[:, 0:D].rearrange("p (h c) -> p h c", h=H),
                                in0=oldrow[:, 0:D].rearrange("p (h c) -> p h c", h=H), in1=heads(f0), op=ALU.mult).then_inc(r["new"], 1)
                v.tensor_tensor(out=newrow[:, SC:SC + H], in0=oldrow[:, SC:SC + H], in1=f0, op=ALU.mult).then_inc(r["new"], 1)
                v.wait_ge(r["new"], 3 * T)
                v.wait_ge(r["car"], T)
                v.tensor_tensor(out=newrow[:, 0:D], in0=psum[:, F0 + 2, 0:D], in1=newrow[:, 0:D], op=ALU.add).then_inc(r["fr"], 1)
                v.tensor_tensor(out=newrow[:, SC:SC + H], in0=psum[:, F0 + 3, 0:H], in1=newrow[:, SC:SC + H], op=ALU.add).then_inc(r["fr"], 1)
            return g_sync, g_scalar, g_gpsimd, g_vector, g_tensor

        nodes = {k: sem(f"n_{k}") for k in ("small", "o", "mn", "ex", "r1", "r2")}
        nodes3 = {k: sem(f"n3_{k}") for k in ("tr", "xT", "mm", "small", "d", "w", "c", "oS", "ob", "oh", "o", "xx")}
        n_x = [sem(f"n_x{b}") for b in range(2)]
        n_t = [sem(f"n_t{b}") for b in range(2)]
        n_w = [sem(f"n_w{b}") for b in range(2)]
        ln_sems = {k: sem(f"ln_{k}") for k in ("st", "mv", "ve", "rs", "y")}

        def node_pass_2():
            fresh()
            H = H2
            HD = D // H
            xt = take([2, J, D])
            tt = take([2, J, TW])
            rs = take([2, J, H])
            o = take([2, J, D])
            ex = take([2, J, D])
            rr = take([J, D])
            y = take([2, J, D])
            ln = Norm(ln_sems)
            r = nodes
            S0 = 0
            S1 = S0 + NS
            lx = n_x
            lt = n_t
            lw = n_w

            def n_sync(sp):
                def store(k):
                    sp.wait_ge(ln.s["y"], J * (k.s + 1))
                    a, n = node_view(x3_d, k, start=S0)
                    sp.dma_start(a, y[0:n, k.b, :, :]).then_inc(lw[k.b], 16)

                def body(k):
                    wait(sp, r["r2"], k.s - 1)
                    a, n = node_view(x2_d, k, start=S0)
                    sp.dma_start(xt[0:n, k.b, :, :], a).then_inc(lx[k.b], 16)
                    a, n = node_view(tab, k, start=S0)
                    sp.dma_start(tt[0:n, k.b, :, :], a).then_inc(lt[k.b], 16)
                    if not (k.known() and k.s < S0 + 3):
                        store(k.plus(-3))
                run_steps(sp, NS, body, S0, peel=4)
                for s in (S1 - 3, S1 - 2, S1 - 1):
                    store(at(s))
                for b in range(2):
                    sp.wait_ge(lw[b], 16 * ((S1 + 1 - b) // 2))

            def n_scalar(act):
                def body(k):
                    act.wait_ge(r["o"], k.s + 1)
                    wait(act, r["r1"], k.s - 1)
                    act.activation(ex[:, k.b, :, :], o[:, k.b, :, :], ACT.Relu, scale=-1.0).then_inc(r["mn"], 1)
                    act.wait_ge(r["mn"], k.s + 1)
                    act.activation(ex[:, k.b, :, :], ex[:, k.b, :, :], ACT.Exp, scale=-1.0).then_inc(r["ex"], 1)
                run_steps(act, NS, body, S0)

            def n_gpsimd(pool):
                def weighted(k):
                    pool.wait_ge(r["small"], 2 * (k.s + 1))
                    wait(pool, r["r1"], k.s - 1)
                    pool.tensor_tensor(out=o[:, k.b, :, :].rearrange("p j (h c) -> p j h c", h=H), in0=tt[:, k.b, :, 0:D].rearrange("p j (h c) -> p j h c", h=H),
                                       in1=rs[:, k.b, :, :].rearrange("p j (h a) -> p j h a", a=1).to_broadcast([P, J, H, HD]), op=ALU.mult).then_inc(r["o"], 1)
                weighted(at(S0))

                def body(k):
                    if live(k.plus(1), S1):
                        weighted(k.plus(1))
                    ln.rstd(pool, k)
                run_steps(pool, NS, body, S0)

            def n_vector(v):
                def small(k):
                    v.wait_ge(lt[k.b], 16 * (k.n + 1))
                    wait(v, r["o"], k.s - 1)
                    link = linker(v, r["small"], k, 2)
                    link(v.tensor_scalar(rs[:, k.b, :, :], tt[:, k.b, :, SC:SC + H], 1e-30, None, ALU.max))
                    link(v.reciprocal(rs[:, k.b, :, :], rs[:, k.b, :, :]))

                def scale(k):
                    wait(v, lw[k.b], 16 * k.n)
                    ln.scale(v, k, rr, y[:, k.b, :, :])
                small(at(S0))

                def body(k):
                    if live(k.plus(1), S1):
                        small(k.plus(1))
                    if not (k.known() and k.s == S0):
                        scale(k.plus(-1))
                    v.wait_ge(r["ex"], k.s + 1)
                    wait(v, ln.s["y"], J * k.s)
                    v.scalar_tensor_tensor(out=rr, in0=o[:, k.b, :, :], scalar=0.0, in1=ex[:, k.b, :, :], op0=ALU.max, op1=ALU.add).then_inc(r["r1"], 1)
                    v.wait_ge(r["r1"], k.s + 1)
                    v.wait_ge(lx[k.b], 16 * (k.n + 1))
                    v.scalar_tensor_tensor(out=rr, in0=rr, scalar=-1.0, in1=xt[:, k.b, :, :], op0=ALU.add, op1=ALU.add).then_inc(r["r2"], 1)
                    v.wait_ge(r["r2"], k.s + 1)
                    ln.stats(v, k, rr)
                run_steps(v, NS, body, S0)
                scale(at(S1 - 1))

            return n_sync, n_scalar, n_gpsimd, n_vector, lambda pe: None

        def node_pass_3():
            fresh()
            H = H3
            HD = D // H
            xt = take([2, J, D])
            tt = take([2, J, TW])
            xT = take([FH, STEP])
            pen = take([J, H])
            Mp = take([J, H])
            l1 = take([J, H])
            l2 = take([J, H])
            es = take([J, H])
            mm_ = take([J, H])
            dd = take([2, J, H])
            ww = take([2, J, H])
            t1 = take([J, H])
            den = take([J, H])
            cc = take([2, J, H])
            oS = take([J, D])
            o = take([2, J, D])
            ex = take([J, D])
            xx = take([2, J, D])
            rr = take([J, D])
            y = take([2, J, D])
            ln = Norm(ln_sems)
            r = dict(nodes, **nodes3)
            S0 = NS
            S1 = S0 + NS
            lx = n_x
            lt = n_t
            lw = n_w

            def n_sync(sp):
                def store(k):
                    sp.wait_ge(ln.s["y"], J * (k.s + 1))
                    a, n = node_view(out, k, start=S0)
                    sp.dma_start(a, y[0:n, k.b, :, :]).then_inc(lw[k.b], 16)

                def body(k):
                    wait(sp, r["tr"], k.s - S0 - 1)
                    wait(sp, r["xx"], k.s - S0 - 1)
                    a, n = node_view(x3_d, k, start=S0)
                    sp.dma_start(xt[0:n, k.b, :, :], a).then_inc(lx[k.b], 16)
                    wait(sp, r["ob"], k.s - S0 - 1)
                    a, n = node_view(tab, k, start=S0)
                    sp.dma_start(tt[0:n, k.b, :, :], a).then_inc(lt[k.b], 16)
                    if not (k.known() and k.s < S0 + 3):
                        store(k.plus(-3))
                run_steps(sp, NS, body, S0, peel=4)
                for s in (S1 - 3, S1 - 2, S1 - 1):
                    store(at(s))
                for b in range(2):
                    sp.wait_ge(lw[b], 16 * ((S1 + 1 - b) // 2))

            def n_tensor(pe):
                def tr(k):
                    pe.wait_ge(lx[k.b], 16 * (k.n + 1))
                    wait(pe, r["xT"], FH * (k.s - S0))
                    for f in range(FH):
                        for j in range(J):
                            last = pe.transpose(psum[:, f, j * P:(j + 1) * P], xt[:, k.b, j, f * P:(f + 1) * P], ident[:, :])
                    last.then_inc(r["tr"], 1)

                def mm(k):
                    pe.wait_ge(r["xT"], FH * (k.s - S0 + 1))
                    wait(pe, r["oh"], k.s - S0)
                    for j in range(J):
                        for f in range(FH):
                            last = pe.matmul(psum[:, 2 + j, 0:D + 2 * H], xT[:, f, j * P:(j + 1) * P], Wg[3][:, f, :], start=(f == 0), stop=(f == FH - 1))
                        last.then_inc(r["mm"], 1)
                tr(at(S0))
                mm(at(S0))
                tr(at(S0 + 1))

                def body(k):
                    if live(k.plus(1), S1):
                        mm(k.plus(1))
                    if live(k.plus(2), S1):
                        tr(k.plus(2))
                run_steps(pe, NS, body, S0)

            def n_scalar(act):
                def evac(k):
                    act.wait_ge(r["tr"], k.s - S0 + 1)
                    wait(act, r["mm"], J * (k.s - S0))
                    for f in range(FH):
                        act.activation(xT[:, f, :], psum[:, f, :], ACT.Copy).then_inc(r["xT"], 1)

                def exps(k):
                    act.wait_ge(r["d"], 2 * (k.s - S0 + 1))
                    wait(act, r["c"], 2 * (k.s - S0))
                    act.activation(ww, dd, ACT.Exp).then_inc(r["w"], 1)

                def twice(k):
                    act.wait_ge(lx[k.b], 16 * (k.n + 1))
                    wait(act, r["r2"], k.s - 1)
                    act.activation(xx[:, k.b, :, :], xt[:, k.b, :, :], ACT.Copy, scale=2.0).then_inc(r["xx"], 1)
                evac(at(S0))
                twice(at(S0))
                exps(at(S0))
                evac(at(S0 + 1))

                def body(k):
                    act.wait_ge(r["o"], k.s - S0 + 1)
                    wait(act, r["r1"], k.s)
                    act.activation(ex, o[:, k.b, :, :], ACT.Relu, scale=-1.0).then_inc(r["mn"], 1)
                    act.wait_ge(r["mn"], k.s + 1)
                    act.activation(ex, ex, ACT.Exp, scale=-1.0).then_inc(r["ex"], 1)
                    if live(k.plus(1), S1):
                        twice(k.plus(1))
                        exps(k.plus(1))
                    if live(k.plus(2), S1):
                        evac(k.plus(2))
                run_steps(act, NS, body, S0)

            def n_gpsimd(pool):
                def weighted(k):
                    pool.wait_ge(r["c"], 2 * (k.s - S0 + 1))
                    wait(pool, r["o"], k.s - S0)
                    pool.tensor_tensor(out=oS.rearrange("p j (h c) -> p j h c", h=H), in0=tt[:, k.b, :, 0:D].rearrange("p j (h c) -> p j h c", h=H),
                                       in1=cc[:, 0, :, :].rearrange("p j (h a) -> p j h a", a=1).to_broadcast([P, J, H, HD]), op=ALU.mult).then_inc(r["oS"], 1)
                    pool.wait_ge(r["oS"], k.s - S0 + 1)
                    pool.tensor_tensor(out=oS, in0=oS, in1=bias3[:, :].rearrange("p (a d) -> p a d", a=1).to_broadcast([P, J, D]), op=ALU.add).then_inc(r["ob"], 1)
                weighted(at(S0))

                def body(k):
                    ln.rstd(pool, k)
                    if live(k.plus(1), S1):
                        weighted(k.plus(1))
                run_steps(pool, NS, body, S0)

            def n_vector(v):
                def factors(k):
                    b = k.b
                    link = linker(v, r["small"], Step(k.s - S0, k.b, k.n), 10)
                    v.wait_ge(lt[b], 16 * (k.n + 1))
                    s, M = tt[:, b, :, SC:SC + H], tt[:, b, :, MC:MC + H]
                    link(v.tensor_scalar(pen, s, 0.0, -BIG, ALU.is_equal, ALU.mult))
                    link(v.tensor_tensor(out=Mp, in0=M, in1=pen, op=ALU.add))
                    v.wait_ge(r["mm"], J * (k.s - S0 + 1))
                    link(v.tensor_copy(l1, psum[:, 2:2 + J, D:D + H]))
                    link(v.tensor_tensor(out=l1, in0=psum[:, 2:2 + J, D + H:D + 2 * H], in1=l1, op=ALU.add))
                    link(v.tensor_scalar(l2, l1, SLOPE, None, ALU.mult))
                    link(v.tensor_tensor(out=es, in0=l1, in1=l2, op=ALU.max))
                    link(v.tensor_tensor(out=mm_, in0=Mp, in1=es, op=ALU.max))
                    wait(v, r["w"], k.s - S0)
                    v.tensor_tensor(out=dd[:, 0, :, :], in0=Mp, in1=mm_, op=ALU.subtract).then_inc(r["d"], 1)
                    v.tensor_tensor(out=dd[:, 1, :, :], in0=es, in1=mm_, op=ALU.subtract).then_inc(r["d"], 1)
                    v.wait_ge(r["w"], k.s - S0 + 1)
                    link(v.tensor_tensor(out=t1, in0=s, in1=ww[:, 0, :, :], op=ALU.mult))
                    link(v.scalar_tensor_tensor(out=den, in0=t1, scalar=1e-16, in1=ww[:, 1, :, :], op0=ALU.add, op1=ALU.add))
                    link(v.reciprocal(den, den))
                    wait(v, r["ob"], k.s - S0)
                    for i in range(2):
                        v.tensor_tensor(out=cc[:, i, :, :], in0=ww[:, i, :, :], in1=den, op=ALU.mult).then_inc(r["c"], 1)
                    v.wait_ge(r["c"], 2 * (k.s - S0 + 1))
                    wait(v, r["r1"], k.s - 1)
                    for j in range(J):
                        last = v.tensor_tensor(out=o[:, b, j, :].rearrange("p (h c) -> p h c", h=H), in0=psum[:, 2 + j, 0:D].rearrange("p (h c) -> p h c", h=H),
                                               in1=cc[:, 1, j, :].rearrange("p (h a) -> p h a", a=1).to_broadcast([P, H, HD]), op=ALU.mult)
                    last.then_inc(r["oh"], 1)

                def scale(k):
                    wait(v, lw[k.b], 16 * k.n)
                    ln.scale(v, k, rr, y[:, k.b, :, :])
                factors(at(S0))

                def body(k):
                    b = k.b
                    v.wait_ge(r["ob"], k.s - S0 + 1)
                    v.wait_ge(r["oh"], k.s - S0 + 1)
                    v.tensor_tensor(out=o[:, b, :, :], in0=o[:, b, :, :], in1=oS, op=ALU.add).then_inc(r["o"], 1)
                    if not (k.known() and k.s == S0):
                        scale(k.plus(-1))
                    v.wait_ge(r["ex"], k.s + 1)
                    wait(v, ln.s["y"], J * k.s)
                    v.scalar_tensor_tensor(out=rr, in0=o[:, b, :, :], scalar=0.0, in1=ex, op0=ALU.max, op1=ALU.add).then_inc(r["r1"], 1)
                    v.wait_ge(r["r1"], k.s + 1)
                    v.wait_ge(r["xx"], k.s - S0 + 1)
                    v.scalar_tensor_tensor(out=rr, in0=rr, scalar=-1.0, in1=xx[:, b, :, :], op0=ALU.add, op1=ALU.add).then_inc(r["r2"], 1)
                    v.wait_ge(r["r2"], k.s + 1)
                    ln.stats(v, k, rr)
                    if live(k.plus(1), S1):
                        factors(k.plus(1))
                run_steps(v, NS, body, S0)
                scale(at(S1 - 1))

            return n_sync, n_scalar, n_gpsimd, n_vector, n_tensor

        PHASES.append(edge_pass(2, x2_d, H2))
        PHASES.append(node_pass_2())
        PHASES.append(edge_pass(3, x3_d, H3))
        PHASES.append(node_pass_3())

        def everything(eng, which):
            for n, phase in enumerate(PHASES[:stop_after]):
                phase[which](eng)
                barrier(eng, n + 1)
            if stop_after < 9 and which == 0:
                eng.wait_ge(s_c['fill1'], 16 * NFILL)
                src_t = {1: tab0[0:N, 0:D], 3: x2_d[0:N, :], 4: tab[0:N, 0:D], 5: x3_d[0:N, :]}[stop_after]
                eng.dma_start(out, src_t).then_inc(s_phase, 16)
                eng.wait_ge(s_phase, 5 * stop_after + 16)

        @block.sync
        def _(sp):
            everything(sp, 0)

        @block.scalar
        def _(act):
            everything(act, 1)

        @block.gpsimd
        def _(pool):
            everything(pool, 2)

        @block.vector
        def _(v):
            everything(v, 3)

        @block.tensor
        def _(pe):
            everything(pe, 4)


_INS = ["x", "src", "dst", "edge_attr_256", "edge_attr_64",
        "L0_gnn_W1", "L0_gnn_b1", "L0_gnn_gamma", "L0_gnn_beta", "L0_gnn_W2", "L0_gnn_b2", "L0_gnn_eps",
        "L1_gnn_u", "L1_gnn_W1", "L1_gnn_b1", "L1_gnn_W2", "L1_gnn_b2",
        "L2_gnn_W", "L2_gnn_attn_l", "L2_gnn_attn_r",
        "L3_gnn_W", "L3_gnn_att_src", "L3_gnn_att_dst", "L3_gnn_bias"]


def kernel(**inputs):
    import numpy as np
    import concourse.bacc as bacc
    from concourse import mybir as mb
    from concourse.bass_utils import run_bass_kernel_spmd

    nc = bacc.Bacc("TRN2", target_bir_lowering=False, num_devices=1)
    arrays, args = {}, []
    for name in _INS:
        a = np.ascontiguousarray(inputs[name])
        arrays[f"in_{name}"] = a
        args.append(nc.dram_tensor(f"in_{name}", a.shape, mb.dt.from_np(a.dtype), kind="ExternalInput").ap())
    out = nc.dram_tensor("out_x", inputs["x"].shape, mb.dt.float32, kind="ExternalOutput").ap()
    gnn_program(nc, *args, out)
    r = run_bass_kernel_spmd(nc, [arrays], core_ids=[0])
    return r.results[0]["out_x"]
```
